# Optimizing a Trainium2 kernel written in Bass

```python
import numpy as np
import jax
import jax.numpy as jnp

def _softmax(x, axis=-1):
    return jax.nn.softmax(x, axis=axis)
def _gelu(x):
    return jax.nn.gelu(x, approximate=True)
def _silu(x):
    return jax.nn.silu(x)
def _sigmoid(x):
    return jax.nn.sigmoid(x)
def _layernorm(x, axis=-1, eps=1e-5):
    m = jnp.mean(x, axis=axis, keepdims=True)
    v = jnp.var(x, axis=axis, keepdims=True)
    return (x - m) / jnp.sqrt(v + eps)
def _scatter_add(tgt, idx, src, axis=0):
    return tgt.at[idx].add(src)
def _segment_sum(src, seg, n):
    return jax.ops.segment_sum(src, seg, n)

kernel_name = 'mk_adj_resnorm_d1_adj_128_1341cc'

def setup_inputs(seed: int = 0):
    np.random.seed(seed)
    _w = jnp.asarray
    def _rec_inputs():
        import jax
        import jax.numpy as jnp
        _gk = jax.random.key(seed)
        x = -0.000929 + 1 * jax.random.normal(jax.random.fold_in(_gk, 1), (8192, 128), jnp.float32)
        _a = jax.random.bernoulli(jax.random.fold_in(_gk, 2), 0.00390625, (8192, 8192))
        _a = jnp.logical_or(_a, jnp.swapaxes(_a, -1, -2))
        _a = jnp.logical_or(_a, jnp.eye(8192, dtype=bool))
        adj = _a.astype(jnp.int32)
        return x, adj
    x, adj = _rec_inputs()
    def _L0_gnn_setup():
        import jax, jax.numpy as jnp
        import numpy as np
        N = 8192
        IN = 128
        OUT = 128
        THR = 0.0001
        ALPHA = 0.2
        NEG = -1000000000.0
        key = jax.random.key(seed)
        k1, k2, k3, k4 = jax.random.split(key, 4)
        inp = jax.random.normal(k1, (N, IN), jnp.float32)
        W = jax.random.normal(k2, (IN, OUT), jnp.float32) * (1.414 * np.sqrt(2.0 / (IN + OUT)))
        a = jax.random.normal(k3, (2 * OUT, 1), jnp.float32) * (1.414 * np.sqrt(2.0 / (2 * OUT + 1)))
        adj = jax.random.randint(k4, (N, N), 0, 2, jnp.int32)
        return {'input': inp, 'W': W, 'a': a, 'adj': adj, 'M': N}
    _L0_gnn_all = _L0_gnn_setup()
    _L0_gnn_in = {k: v for k, v in _L0_gnn_all.items() if k in ('W', 'a', )}
    del _L0_gnn_all

    return {
        "x": x,
        "adj": adj,
        "L0_gnn_W": _L0_gnn_in["W"],
        "L0_gnn_a": _L0_gnn_in["a"],
    }

def reference(x, adj, L0_gnn_W, L0_gnn_a):
    import jax
    import jax.numpy as jnp
    def _L0_gnn_ref(input, W, a, adj, M):
        import jax, jax.numpy as jnp
        import numpy as np
        N = 8192
        IN = 128
        OUT = 128
        THR = 0.0001
        ALPHA = 0.2
        NEG = -1000000000.0
        h = input @ W
        a_src = a[:OUT, 0]
        a_dst = a[OUT:, 0]
        e = jax.nn.leaky_relu((h[:M] @ a_src)[:, None] + (h @ a_dst)[None, :], negative_slope=ALPHA)
        valid = (adj[:M] > 0) & (h.sum(axis=1) != 0)[None, :]
        att = jax.nn.softmax(jnp.where(valid, e, NEG), axis=1)
        att = jnp.where(valid, att, 0.0)
        L = valid.sum(axis=1).astype(h.dtype)
        top = att.max(axis=1)
        attention = jnp.where(att >= THR, att, 0.0) * L[:, None]
        attention = jnp.where((top > THR)[:, None], attention, 0.0)
        h_prime = attention @ h
        return jax.nn.elu(h[:M] + h_prime)

    x = _layernorm(x + _L0_gnn_ref(x, L0_gnn_W, L0_gnn_a, adj, 8192), axis=-1)
    return x


_drawn_inputs = setup_inputs


def setup_inputs(seed=0):
    import zlib

    import numpy as np

    out = dict(_drawn_inputs(seed))
    spreads = {}
    factors = {}
    for name, (base, spread) in spreads.items():
        noise = np.random.default_rng([zlib.crc32(name.encode()), seed]).standard_normal(out[name].shape)
        drawn = base * np.exp(spread * noise) if base else spread * noise
        out[name] = jnp.asarray(drawn.astype(out[name].dtype))
    for name, factor in factors.items():
        out[name] = (out[name] * factor).astype(out[name].dtype)
    return out
```

```python
import concourse.bass as bass
from concourse import mybir
from contextlib import ExitStack


def graph_attention_layer(nc, x, adj, W, a, out):
    fp32, u8, i32 = mybir.dt.float32, mybir.dt.uint8, mybir.dt.int32
    ALU = mybir.AluOpType
    ACT = mybir.ActivationFunctionType
    AX = mybir.AxisListType

    N, F = x.shape
    P = 128
    NT = N // P
    CH = 2048
    NCH = N // CH
    GB = 8
    GC = GB * P
    NG = N // GC
    GPC = CH // GC
    NTR = 2
    AHEAD = 3
    NPT = 4
    XB = 4
    XC = XB * P
    NX = NT // XB
    ALPHA, THR, EPS = 0.2, 1e-4, 1e-5
    BIG = float(2 ** 60)

    x_tiles = x.rearrange("(t p) f -> t p f", p=P)
    x_steps = x.rearrange("(s t p) f -> s p t f", t=XB, p=P)
    adj_tiles = adj.rearrange("(t p) n -> t p n", p=P)
    out_tiles = out.rearrange("(t p) f -> t p f", p=P)

    ctx = ExitStack()
    with ctx:
        def sb(name, shape, dt=fp32):
            return ctx.enter_context(nc.sbuf_tensor(name, shape, dt))

        def sem(name):
            return ctx.enter_context(nc.semaphore(name))

        ident = sb("ident", [P, P])
        ones = sb("ones", [P, P])
        W_sb = sb("W_sb", [P, F])
        WT_sb = sb("WT_sb", [P, P])
        a3 = sb("a3", [P, 3])
        Wa = sb("Wa", [P, 3])
        Wdst = sb("Wdst", [P, P])
        Wsum = sb("Wsum", [P, P])
        h_sb = sb("h_sb", [P, NT, F])
        s_col = sb("s_col", [P, NT, 3])
        q_row = sb("q_row", [P, N])
        adj_sb = sb("adj_sb", [P, NCH, CH], i32)
        w_sb = sb("w_sb", [P, 2, CH])
        p_sb = sb("p_sb", [P, 2, N])
        pT = sb("pT", [P, NPT, GC])
        x_in = pT[:, 0, :].rearrange("p (s t f) -> p s t f", s=2, t=XB)
        xT = pT[:, 1, :].rearrange("p (s c) -> p s c", s=2)
        n_inv = sb("n_inv", [P, 2, NCH])
        q_min = sb("q_min", [P, NX])
        K_sb = sb("K_sb", [P, 2])
        r_bias = sb("r_bias", [P, NT])
        max_c = sb("max_c", [P, 2, NCH])
        row_max = sb("row_max", [P, 2])
        shift = sb("shift", [P, 2])
        dead_row = p_sb[:, 1, :]
        sum_c = sb("sum_c", [P, 2, NCH])
        stats = sb("stats", [P, 2, 4])
        gate = sb("gate", [P, 2, 3])
        g_sb = sb("g_sb", [P, 2, F])
        neg = sb("neg", [P, 2, F])
        e_neg = sb("e_neg", [P, 2, F])
        x_res = sb("x_res", [P, 2, F])
        y_sb = sb("y_sb", [P, 2, F])
        elu = sb("elu", [P, F])
        moments = sb("moments", [P, 2, 6])
        eps = sb("eps", [P, 1])
        ln = sb("ln", [P, 2, 6])
        rs = sb("rs", [P, 2, 3])
        o_sb = sb("o_sb", [P, 2, F])

        tr_ps = [ctx.enter_context(nc.psum_tensor(f"tr_ps{i}", [P, GC], fp32)) for i in range(NTR)]
        acc_ps = [ctx.enter_context(nc.psum_tensor(f"acc_ps{i}", [P, 512], fp32)) for i in range(2)]
        h_ps = ctx.enter_context(nc.psum_tensor("h_ps", [P, 512], fp32))
        s_ps = ctx.enter_context(nc.psum_tensor("s_ps", [P, 512], fp32))
        xT_ps, d_ps = tr_ps[0][:, 0:512], tr_ps[0][:, 512:1024]
        sum_ps = tr_ps[1][:, 0:512]
        w_ps = acc_ps[0]

        passed = sem("passed")
        consts_zeroed = sem("consts_zeroed")
        consts_ready = sem("consts_ready")
        weights_loaded = sem("weights_loaded")
        WT_done = sem("WT_done")
        WT_copied = sem("WT_copied")
        Wa_done = sem("Wa_done")
        Wa_copied = sem("Wa_copied")
        W_ready = sem("W_ready")
        xin_loaded = [sem(f"xin_loaded{i}") for i in range(2)]
        xT_done = sem("xT_done")
        xT_copied = sem("xT_copied")
        first_mm = sem("first_mm")
        rows_copied = sem("rows_copied")
        h_copied = sem("h_copied")
        adj_loaded = [sem(f"adj_loaded{c}") for c in range(NCH)]
        adj_used = sem("adj_used")
        inv_ready = sem("inv_ready")
        masked_ready = sem("masked_ready")
        rowmax_ready = sem("rowmax_ready")
        qmin_done = sem("qmin_done")
        K_ready = sem("K_ready")
        q_ready = sem("q_ready")
        bias_ready = sem("bias_ready")
        shift_ready = sem("shift_ready")
        relu_done = sem("relu_done")
        exp_done = sem("exp_done")
        stats_link = sem("stats_link")
        stats_ready = sem("stats_ready")
        gate_link = sem("gate_link")
        gate_ready = sem("gate_ready")
        thr_done = sem("thr_done")
        tr_done = sem("tr_done")
        evac_done = sem("evac_done")
        mm_done = sem("mm_done")
        g_ready = sem("g_ready")
        neg_ready = sem("neg_ready")
        eneg_ready = sem("eneg_ready")
        xres_loaded = [sem(f"xres_loaded{i}") for i in range(2)]
        y_link = sem("y_link")
        y_ready = sem("y_ready")
        moments_ready = sem("moments_ready")
        var_ready = sem("var_ready")
        log_ready = sem("log_ready")
        rs_ready = sem("rs_ready")
        out_link = sem("out_link")
        out_stored = [sem(f"out_stored{i}") for i in range(2)]

        block = ctx.enter_context(nc.Block())

        def wait_apart(eng, *waits):
            for semaphore, value in waits:
                eng.wait_ge(semaphore, value)
            eng.sem_inc(passed, 1)

        def slots(eng, slot, last_lag, ahead=0, head=4):
            def straight(k):
                slot(k, k % 2, lambda lag: 0 <= k - lag < NT)

            for k in range(head):
                straight(k)
            with eng.Fori(head // 2, NT // 2 - ahead) as i:
                for u in range(2):
                    slot(i * 2 + u, u, lambda lag: True)
            for k in range(NT - 2 * ahead, NT + last_lag):
                straight(k)

        @block.sync
        def _(sp):
            sp.dma_start(W_sb[:, :], W).then_inc(weights_loaded, 16)
            sp.dma_start(a3[:, 0:1], a[0:F, :]).then_inc(weights_loaded, 16)
            sp.dma_start(a3[:, 1:2], a[F:2 * F, :]).then_inc(weights_loaded, 16)
            for s in range(2):
                sp.dma_start(x_in[:, s, :, :], x_steps[s]).then_inc(xin_loaded[s], 16)
            for c in range(NCH):
                sp.dma_start(adj_sb[:, c, :], adj_tiles[0, :, c * CH:(c + 1) * CH])\
                  .then_inc(adj_loaded[c], 16)
            with sp.Fori(1, NX // 2) as i:
                for u in range(2):
                    sp.wait_ge(xT_done, i * 2 + (u - 1))
                    sp.dma_start(x_in[:, u, :, :], x_steps[bass.ds(i * 2 + u, 1)].rearrange("s p t f -> p (s t) f"))\
                      .then_inc(xin_loaded[u], 16)
            with sp.Fori(1, NT) as k:
                for c in range(NCH):
                    sp.wait_ge(adj_used, k * NCH + (c + 1 - NCH))
                    sp.dma_start(adj_sb[:, c, :],
                                 adj_tiles[bass.ds(k, 1), :, c * CH:(c + 1) * CH]
                                 .rearrange("t p n -> (t p) n"))\
                      .then_inc(adj_loaded[c], 16)

        @block.gpsimd
        def _(pool):
            nc.gpsimd.memset(ident[:, :], 0.0).then_inc(consts_zeroed, 1)
            nc.gpsimd.memset(ones[:, :], 1.0).then_inc(consts_ready, 1)
            nc.gpsimd.memset(a3[:, 2:3], 1.0).then_inc(consts_ready, 1)
            nc.gpsimd.memset(eps[:, :], EPS).then_inc(consts_ready, 1)
            pool.wait_ge(consts_zeroed, 1)
            nc.gpsimd.affine_select(out=ident[:, :], in_=ident[:, :], compare_op=ALU.not_equal,
                                    fill=1.0, base=0, pattern=[[-1, P]], channel_multiplier=1)\
              .then_inc(consts_ready, 1)

            def slot(k, u, live):
                v = 1 - u
                if live(0):
                    pool.wait_ge(exp_done, (k + 1) * NCH)
                    nc.gpsimd.tensor_tensor(sum_c[:, u, 0:2], sum_c[:, u, 0:2], sum_c[:, u, 2:4],
                                            ALU.add).then_inc(stats_link, 1)
                    nc.gpsimd.tensor_tensor(n_inv[:, u, 0:2], n_inv[:, u, 0:2], n_inv[:, u, 2:4],
                                            ALU.add).then_inc(stats_link, 1)
                    pool.wait_ge(stats_link, k * 4 + 2)
                    nc.gpsimd.tensor_tensor(stats[:, u, 0:1], sum_c[:, u, 0:1], sum_c[:, u, 1:2],
                                            ALU.add).then_inc(stats_link, 1)
                    nc.gpsimd.tensor_tensor(stats[:, u, 2:3], n_inv[:, u, 0:1], n_inv[:, u, 1:2],
                                            ALU.add).then_inc(stats_link, 1)
                    wait_apart(pool, (stats_link, k * 4 + 4))
                    nc.gpsimd.tensor_scalar(stats[:, u, 3:4], stats[:, u, 2:3], -1.0, float(N),
                                            ALU.mult, ALU.add).then_inc(stats_ready, 1)
                    nc.gpsimd.tensor_scalar(stats[:, u, 1:2], stats[:, u, 0:1], THR, 0.0,
                                            ALU.mult, ALU.add).then_inc(stats_ready, 1)
                if live(2):
                    if not isinstance(k, int) or k >= 4:
                        pool.wait_ge(y_ready, k - 3)
                    pool.dma_start(x_res[:, u, :], x_tiles[bass.ds(k - 2, 1)]
                                   .rearrange("t p f -> (t p) f")).then_inc(xres_loaded[u], 16)
                    wait_apart(pool, (g_ready, k - 1))
                    nc.gpsimd.tensor_scalar(neg[:, u, :], g_sb[:, u, :], 0.0, 0.0, ALU.min, ALU.add)\
                      .then_inc(neg_ready, 1)
                if live(3):
                    j = k - 3
                    nc.gpsimd.tensor_scalar(elu[:, :], g_sb[:, v, :], 0.0, -1.0, ALU.max, ALU.add)\
                      .then_inc(y_link, 1)
                    pool.wait_ge(y_link, j * 2 + 1)
                    pool.wait_ge(eneg_ready, k - 2)
                    nc.gpsimd.tensor_tensor(elu[:, :], elu[:, :], e_neg[:, v, :], ALU.add)\
                      .then_inc(y_link, 1)
                    pool.wait_ge(y_link, j * 2 + 2)
                    if isinstance(k, int):
                        pool.wait_ge(xres_loaded[v], 16 * (j // 2 + 1))
                    else:
                        pool.wait_ge(xres_loaded[v], (j + (1 if u == 0 else 2)) * 8)
                    nc.gpsimd.tensor_tensor(y_sb[:, v, :], elu[:, :], x_res[:, v, :], ALU.add)\
                      .then_inc(y_ready, 1)
                if live(4):
                    j = k - 4
                    pool.wait_ge(rs_ready, k - 3)
                    nc.gpsimd.tensor_tensor(ln[:, u, 2:3], rs[:, u, 1:2], rs[:, u, 1:2], ALU.mult)\
                      .then_inc(out_link, 1)
                    pool.wait_ge(out_link, j * 5 + 1)
                    nc.gpsimd.tensor_tensor(ln[:, u, 3:4], ln[:, u, 2:3], rs[:, u, 2:3], ALU.mult)\
                      .then_inc(out_link, 1)
                    wait_apart(pool, (out_link, j * 5 + 2))
                    nc.gpsimd.tensor_scalar(ln[:, u, 4:5], ln[:, u, 3:4], -0.5, 1.5,
                                            ALU.mult, ALU.add).then_inc(out_link, 1)
                    pool.wait_ge(out_link, j * 5 + 3)
                    nc.gpsimd.tensor_tensor(ln[:, u, 5:6], ln[:, u, 4:5], rs[:, u, 1:2], ALU.mult)\
                      .then_inc(out_link, 1)
                    if not isinstance(k, int):
                        wait_apart(pool, (out_link, j * 5 + 4), (out_stored[u], (j - u) * 8))
                    else:
                        pool.wait_ge(out_link, j * 5 + 4)
                        if j >= 2:
                            pool.wait_ge(out_stored[u], 16 * (j // 2))
                    nc.gpsimd.tensor_scalar(o_sb[:, u, :], y_sb[:, u, :], ln[:, u, 0:1], ln[:, u, 5:6],
                                            ALU.subtract, ALU.mult).then_inc(out_link, 1)
                    pool.wait_ge(out_link, j * 5 + 5)
                    pool.dma_start(out_tiles[bass.ds(j, 1)].rearrange("t p f -> (t p) f"),
                                   o_sb[:, u, :]).then_inc(out_stored[u], 16)

            slots(pool, slot, 4, head=6)
            for u in range(2):
                pool.wait_ge(out_stored[u], 16 * (NT // 2))

        @block.scalar
        def _(act):
            nc.scalar.preload_act_table_set("natural_log_exp_and_others")
            act.wait_ge(consts_ready, 4)
            act.wait_ge(WT_done, 1)
            nc.scalar.copy(WT_sb[:, :], w_ps[:, 0:P]).then_inc(WT_copied, 1)
            act.wait_ge(Wa_done, 1)
            nc.scalar.copy(Wa[:, :], w_ps[:, 128:131]).then_inc(Wa_copied, 1)
            act.wait_ge(Wa_copied, 1)
            nc.scalar.mul(Wdst[:, :], ones[:, :], Wa[:, 1:2]).then_inc(W_ready, 1)
            nc.scalar.mul(Wsum[:, :], ones[:, :], Wa[:, 2:3]).then_inc(W_ready, 1)
            def first(s, u, peeled):
                act.wait_ge(xT_done, s + 1)
                if not peeled:
                    act.wait_ge(first_mm, s - 1)
                nc.scalar.copy(xT[:, u, :], xT_ps).then_inc(xT_copied, 1)
                act.wait_ge(first_mm, s + 1)
                nc.scalar.mul(q_row[:, bass.ds(s * XC, XC)], d_ps, -ALPHA / BIG).then_inc(rows_copied, 1)
            for s in range(2):
                first(s, s, True)
            with act.Fori(1, NX // 2) as i:
                for u in range(2):
                    first(i * 2 + u, u, False)

            def relu(k, u, c):
                nc.scalar.activation(p_sb[:, u, c * CH:(c + 1) * CH], q_row[:, c * CH:(c + 1) * CH],
                                     ACT.Relu, bias=r_bias[:, bass.ds(k, 1)],
                                     scale=-(1 - ALPHA) / ALPHA).then_inc(relu_done, 1)

            act.wait_ge(q_ready, NCH)
            act.wait_ge(bias_ready, 1)
            for c in range(NCH):
                relu(0, 0, c)

            def exp(k, u, c):
                pc = p_sb[:, u, c * CH:(c + 1) * CH]
                nc.scalar.activation(pc, pc, ACT.Exp, bias=shift[:, u:u + 1],
                                     accum_out=sum_c[:, u, c:c + 1]).then_inc(exp_done, 1)

            def evac(k, g):
                n = k * NG + g
                act.wait_ge(tr_done, n + 1)
                if not isinstance(n, int) or n >= NPT:
                    act.wait_ge(mm_done, n + (1 - NPT))
                nc.scalar.copy(pT[:, g % NPT, :], tr_ps[g % NTR][:, :]).then_inc(evac_done, 1)

            def slot(k, u, live):
                v = 1 - u
                if live(0):
                    act.wait_ge(rowmax_ready, k + 1)
                    nc.scalar.mul(shift[:, u:u + 1], row_max[:, u:u + 1], -1.0).then_inc(shift_ready, 1)
                    act.wait_ge(shift_ready, k + 1)
                    exp(k, u, 0)
                for c in range(NCH):
                    if live(0) and c + 1 < NCH:
                        exp(k, u, c + 1)
                    if live(1):
                        for g in range(c * GPC, (c + 1) * GPC):
                            evac(k - 1, g)
                    if live(-1):
                        relu(k + 1, v, c)
                if live(3):
                    act.wait_ge(neg_ready, k - 2)
                    nc.scalar.activation(e_neg[:, v, :], neg[:, v, :], ACT.Exp).then_inc(eneg_ready, 1)
                if live(4):
                    act.wait_ge(var_ready, k - 3)
                    nc.scalar.activation(rs[:, u, 2:3], ln[:, u, 1:2], ACT.Identity, bias=eps[:, :])\
                      .then_inc(log_ready, 1)
                    act.wait_ge(log_ready, (k - 4) * 2 + 1)
                    nc.scalar.activation(rs[:, u, 0:1], rs[:, u, 2:3], ACT.Ln).then_inc(log_ready, 1)
                    act.wait_ge(log_ready, (k - 3) * 2)
                    nc.scalar.activation(rs[:, u, 1:2], rs[:, u, 0:1], ACT.Exp, scale=-0.5)\
                      .then_inc(rs_ready, 1)

            slots(act, slot, 4, ahead=1)

        @block.vector
        def _(dve):
            def first(s):
                dve.wait_ge(first_mm, s + 1)
                nc.vector.tensor_copy(h_sb[:, bass.ds(s * XB, XB), :],
                                      h_ps[:, :].rearrange("p (t f) -> p t f", t=XB)).then_inc(h_copied, 1)
                nc.vector.tensor_copy(s_col[:, bass.ds(s * XB, XB), :],
                                      s_ps[:, 0:3 * XB].rearrange("p (t f) -> p t f", t=XB))\
                  .then_inc(h_copied, 1)
                nc.vector.tensor_scalar(dead_row[:, bass.ds(s * XC, XC)], sum_ps, 0.0, None,
                                        ALU.is_equal).then_inc(h_copied, 1)
                dve.wait_ge(rows_copied, s + 1)
                nc.vector.tensor_reduce(q_min[:, bass.ds(s, 1)], q_row[:, bass.ds(s * XC, XC)], AX.X,
                                        ALU.min).then_inc(qmin_done, 1)
            with dve.Fori(0, NX) as s:
                first(s)
            dve.wait_ge(qmin_done, NX)
            nc.vector.tensor_reduce(K_sb[:, 1:2], q_min[:, :], AX.X, ALU.min).then_inc(K_ready, 1)
            dve.wait_ge(K_ready, 1)
            nc.vector.tensor_scalar(K_sb[:, 0:1], K_sb[:, 1:2], -1.0, None, ALU.mult).then_inc(K_ready, 1)
            dve.wait_ge(K_ready, 2)
            nc.vector.tensor_scalar(K_sb[:, 1:2], K_sb[:, 0:1], (1 - ALPHA) / ALPHA, None,
                                    ALU.mult).then_inc(K_ready, 1)
            dve.wait_ge(h_copied, NX * 3)
            for c in range(NCH):
                cols = slice(c * CH, (c + 1) * CH)
                nc.vector.scalar_tensor_tensor(out=q_row[:, cols], in0=q_row[:, cols],
                                               scalar=K_sb[:, 0:1], in1=dead_row[:, cols],
                                               op0=ALU.add, op1=ALU.max).then_inc(q_ready, 1)
            dve.wait_ge(K_ready, 3)
            nc.vector.tensor_scalar(r_bias[:, :], s_col[:, :, 0:1].rearrange("p t a -> p (t a)"),
                                    (1 - ALPHA) / BIG, K_sb[:, 1:2], ALU.mult, ALU.add)\
              .then_inc(bias_ready, 1)
            dve.wait_ge(q_ready, NCH)
            dve.wait_ge(bias_ready, 1)

            def slot(k, u, live):
                v = 1 - u
                if live(0):
                    for c in range(NCH):
                        n = k * NCH + c
                        cols = slice(c * CH, (c + 1) * CH)
                        dve.wait_ge(adj_loaded[c], (k + 1) * 16)
                        nc.vector.scalar_tensor_tensor(
                            out=w_sb[:, c % 2, :], in0=adj_sb[:, c, :], scalar=0.0,
                            in1=q_row[:, cols], op0=ALU.is_le, op1=ALU.max,
                            accum_out=n_inv[:, u, c:c + 1]).then_inc(adj_used, 1)
                        wait_apart(dve, (adj_used, n + 1), (relu_done, n + 1))
                        nc.vector.tensor_tensor_reduce(
                            out=p_sb[:, u, cols], in0=p_sb[:, u, cols], in1=w_sb[:, c % 2, :],
                            scale=BIG, scalar=-4.0 * BIG, op0=ALU.subtract, op1=ALU.max,
                            accum_out=max_c[:, u, c:c + 1]).then_inc(masked_ready, 1)
                    dve.wait_ge(masked_ready, (k + 1) * NCH)
                    nc.vector.tensor_reduce(row_max[:, u:u + 1], max_c[:, u, :], AX.X, ALU.max)\
                      .then_inc(rowmax_ready, 1)
                if live(1):
                    dve.wait_ge(stats_ready, k * 2)
                    nc.vector.reciprocal(gate[:, v, 0:1], stats[:, v, 0:1]).then_inc(gate_link, 1)
                    for c in range(NCH):
                        pc = p_sb[:, v, c * CH:(c + 1) * CH]
                        nc.vector.scalar_tensor_tensor(out=pc, in0=pc, scalar=stats[:, v, 1:2], in1=pc,
                                                       op0=ALU.is_ge, op1=ALU.mult).then_inc(thr_done, 1)
                        if c == 0:
                            dve.wait_ge(gate_link, k * 2 - 1)
                            nc.vector.scalar_tensor_tensor(
                                out=gate[:, v, 1:2], in0=gate[:, v, 0:1], scalar=THR,
                                in1=stats[:, v, 3:4], op0=ALU.is_gt, op1=ALU.mult).then_inc(gate_link, 1)
                        if c == 1:
                            dve.wait_ge(gate_link, k * 2)
                            nc.vector.tensor_tensor(gate[:, v, 2:3], gate[:, v, 1:2], gate[:, v, 0:1],
                                                    ALU.mult).then_inc(gate_ready, 1)
                if live(2):
                    dve.wait_ge(mm_done, (k - 1) * NG)
                    dve.wait_ge(gate_ready, k - 1)
                    if not isinstance(k, int) or k >= 4:
                        dve.wait_ge(y_link, (k - 3) * 2)
                    nc.vector.scalar_tensor_tensor(
                        out=g_sb[:, u, :], in0=acc_ps[u][:, 0:F], scalar=gate[:, u, 2:3],
                        in1=h_sb[:, bass.ds(k - 2, 1), :].rearrange("p a f -> p (a f)"),
                        op0=ALU.mult, op1=ALU.add).then_inc(g_ready, 1)

                if live(4):
                    dve.wait_ge(y_ready, k - 3)
                    nc.vector.bn_stats(moments[:, u, :], y_sb[:, u, :]).then_inc(moments_ready, 1)
                    wait_apart(dve, (moments_ready, k - 3))
                    nc.vector.bn_aggr(ln[:, u, 0:2], moments[:, u, :]).then_inc(var_ready, 1)

            slots(dve, slot, 4)

        @block.tensor
        def _(pe):
            pe.wait_ge(consts_ready, 4)
            pe.wait_ge(weights_loaded, 48)
            nc.tensor.transpose(w_ps[:, 0:P], W_sb[:, :], ident[:, :]).then_inc(WT_done, 1)
            pe.wait_ge(WT_copied, 1)
            nc.tensor.matmul(w_ps[:, 128:131], WT_sb[:, :], a3[:, :], start=True, stop=True)\
              .then_inc(Wa_done, 1)
            pe.wait_ge(W_ready, 2)

            def first(s, u, peeled):
                pe.wait_ge(xin_loaded[u], 16 if peeled else (s - u) * 8 + 16)
                if not peeled or s >= 1:
                    pe.wait_ge(xT_copied, s)
                for t in range(XB):
                    last = nc.tensor.transpose(xT_ps[:, t * P:(t + 1) * P], x_in[:, u, t, :], ident[:, :])
                last.then_inc(xT_done, 1)
                pe.wait_ge(xT_copied, s + 1)
                if not peeled or s >= 1:
                    pe.wait_ge(rows_copied, s)
                    pe.wait_ge(h_copied, s * 3)
                for t in range(XB):
                    xt = xT[:, u, t * P:(t + 1) * P]
                    nc.tensor.matmul(h_ps[:, t * P:(t + 1) * P], xt, W_sb[:, :], start=True, stop=True)
                    nc.tensor.matmul(s_ps[:, 3 * t:3 * t + 3], xt, Wa[:, :], start=True, stop=True)
                nc.tensor.matmul(sum_ps, Wsum[:, :], xT[:, u, :], start=True, stop=True)
                nc.tensor.matmul(d_ps, Wdst[:, :], xT[:, u, :], start=True, stop=True).then_inc(first_mm, 1)
            for s in range(2):
                first(s, s, True)
            with pe.Fori(1, NX // 2) as i:
                for u in range(2):
                    first(i * 2 + u, u, False)
            pe.wait_ge(h_copied, NX * 3)
            pe.wait_ge(rows_copied, NX)

            def tile(k, u, peeled):
                def transposes(g):
                    n = k * NG + g
                    if g % GPC == 0:
                        pe.wait_ge(thr_done, k * NCH + (g // GPC + 1))
                    if not peeled or n >= NTR:
                        pe.wait_ge(evac_done, n + (1 - NTR))
                    for b in range(GB):
                        at = g * GC + b * P
                        last = nc.tensor.transpose(tr_ps[g % NTR][:, b * P:(b + 1) * P],
                                                   p_sb[:, u, at:at + P], ident[:, :])
                    last.then_inc(tr_done, 1)

                def products(g):
                    pe.wait_ge(evac_done, k * NG + (g + 1))
                    if g == 0 and (not peeled or k >= 2):
                        pe.wait_ge(g_ready, k - 1)
                    for b in range(GB):
                        j = g * GB + b
                        last = nc.tensor.matmul(acc_ps[u][:, 0:F], pT[:, g % NPT, b * P:(b + 1) * P],
                                                h_sb[:, j, :], start=(j == 0), stop=(j == NT - 1))
                    last.then_inc(mm_done, 1)

                for g in range(NG + AHEAD):
                    if g < NG:
                        transposes(g)
                    if g >= AHEAD:
                        products(g - AHEAD)

            for k in range(2):
                tile(k, k, True)
            with pe.Fori(1, NT // 2) as i:
                for u in range(2):
                    tile(i * 2 + u, u, False)


_INS = ["x", "adj", "L0_gnn_W", "L0_gnn_a"]


def kernel(**inputs):
    import numpy as _np
    import concourse.bacc as _bacc
    from concourse import mybir as _mybir
    from concourse.bass_utils import run_bass_kernel_spmd as _run

    nc = _bacc.Bacc("TRN2", target_bir_lowering=False, num_devices=1)
    arrays, args = {}, []
    for name in _INS:
        array = _np.ascontiguousarray(inputs[name])
        arrays[f"in_{name}"] = array
        args.append(nc.dram_tensor(f"in_{name}", array.shape, _mybir.dt.from_np(array.dtype),
                                   kind="ExternalInput").ap())
    shape = inputs["x"].shape
    out = nc.dram_tensor("out_dram", shape, _mybir.dt.float32, kind="ExternalOutput").ap()
    graph_attention_layer(nc, *args, out)
    r = _run(nc, [arrays], core_ids=[0])
    return r.results[0]["out_dram"]
```

```python
import concourse.bass as bass
from concourse import mybir
from contextlib import ExitStack


def graph_attention_layer(nc, x, adj, W, a, q_dram, out):
    fp32, u8, i32 = mybir.dt.float32, mybir.dt.uint8, mybir.dt.int32
    ALU = mybir.AluOpType
    ACT = mybir.ActivationFunctionType
    AX = mybir.AxisListType

    N, F = x.shape
    P = 128
    F3 = F + 3
    NT = N // P
    CH = 2048
    NCH = N // CH
    GB = 8
    GC = GB * P
    NG = N // GC
    GPC = CH // GC
    NTR = 2
    AHEAD = 3
    NPT = 4
    XB = 4
    XC = XB * P
    NX = NT // XB
    NXB = 4
    ALPHA, THR, EPS = 0.2, 1e-4, 1e-5
    BIG = float(2 ** 60)

    x_tiles = x.rearrange("(t p) f -> t p f", p=P)
    x_steps = x.rearrange("(s t p) f -> s p t f", t=XB, p=P)
    q_flat = q_dram.rearrange("t p -> (t p)")
    adj_tiles = adj.rearrange("(t p) n -> t p n", p=P)
    out_tiles = out.rearrange("(t p) f -> t p f", p=P)

    ctx = ExitStack()
    with ctx:
        def sb(name, shape, dt=fp32):
            return ctx.enter_context(nc.sbuf_tensor(name, shape, dt))

        def sem(name):
            return ctx.enter_context(nc.semaphore(name))

        ident = sb("ident", [P, P])
        ones = sb("ones", [1, P])
        W_sb = sb("W_sb", [P, F3])
        WT_sb = sb("WT_sb", [P, P])
        a3 = sb("a3", [P, 3])
        h_sb = sb("h_sb", [P, NT, F3])
        s_col, d_col, sum_col = (h_sb[:, :, F + i:F + i + 1].rearrange("p t a -> p (t a)")
                                 for i in range(3))
        q_row = sb("q_row", [P, N])
        adj_sb = sb("adj_sb", [P, NCH, CH], i32)
        w_sb = sb("w_sb", [P, 2, CH])
        p_sb = sb("p_sb", [P, 2, N])
        pT = sb("pT", [P, NPT, GC])
        xT = pT[:, 0, :].rearrange("p (s c) -> p s c", s=2)
        x_in = p_sb[:, 1, 0:NXB * XC].rearrange("p (s t f) -> p s t f", s=NXB, t=XB)
        n_inv = sb("n_inv", [P, 2, NCH])
        d_max = sb("d_max", [P, 2])
        K_sb = sb("K_sb", [P, 2])
        q_col = sb("q_col", [P, NT])
        qT_sb = sb("qT_sb", [NT, P])
        r_bias = sb("r_bias", [P, NT])
        max_c = sb("max_c", [P, 2, NCH])
        row_max = sb("row_max", [P, 2])
        shift = sb("shift", [P, 2])
        sum_c = sb("sum_c", [P, 2, NCH])
        stats = sb("stats", [P, 2, 3])
        addends = sb("addends", [P, 2, 3, NCH])
        gate = sb("gate", [P, 2, 3])
        g_sb = sb("g_sb", [P, 2, F])
        neg = sb("neg", [P, 2, F])
        e_neg = sb("e_neg", [P, 2, F])
        x_res = sb("x_res", [P, 2, F])
        y_sb = sb("y_sb", [P, 2, F])
        elu = sb("elu", [P, 2, 2, F])
        moments = sb("moments", [P, 2, 6])
        consts = sb("consts", [P, 4])
        ln = sb("ln", [P, 2, 2])
        rs = sb("rs", [P, 2, 7])
        o_sb = sb("o_sb", [P, 2, F])

        tr_ps = [ctx.enter_context(nc.psum_tensor(f"tr_ps{i}", [P, GC], fp32)) for i in range(NTR)]
        acc_ps = [ctx.enter_context(nc.psum_tensor(f"acc_ps{i}", [P, 512], fp32)) for i in range(2)]
        h_ps = [ctx.enter_context(nc.psum_tensor(f"h_ps{i}", [P, 512], fp32)) for i in range(2)]
        xT_ps = [tr_ps[i][:, 0:512] for i in range(2)]
        hs_ps = [[h_ps[i][:, 0:2 * F3], tr_ps[i][:, 512:512 + 2 * F3]] for i in range(2)]
        k_ps = acc_ps[1]
        w_ps = acc_ps[0]

        passed = sem("passed")
        consts_zeroed = sem("consts_zeroed")
        consts_ready = sem("consts_ready")
        weights_loaded = sem("weights_loaded")
        WT_done = sem("WT_done")
        WT_copied = sem("WT_copied")
        Wa_done = sem("Wa_done")
        Wa_copied = sem("Wa_copied")
        x_loaded = [sem(f"x_loaded{i}") for i in range(NXB)]
        xT_done = sem("xT_done")
        xT_copied = sem("xT_copied")
        first_mm = sem("first_mm")
        h_copied = sem("h_copied")
        adj_loaded = [sem(f"adj_loaded{c}") for c in range(NCH)]
        adj_used = sem("adj_used")
        inv_ready = sem("inv_ready")
        masked_ready = sem("masked_ready")
        rowmax_ready = sem("rowmax_ready")
        dmax_done = sem("dmax_done")
        dmaxT_done = sem("dmaxT_done")
        dtop_done = sem("dtop_done")
        dtop_spread = sem("dtop_spread")
        K_ready = sem("K_ready")
        q_link = sem("q_link")
        qT_done = sem("qT_done")
        qT_copied = sem("qT_copied")
        q_stored = sem("q_stored")
        q_loaded = [sem(f"q_loaded{c}") for c in range(NCH)]
        bias_ready = sem("bias_ready")
        shift_ready = sem("shift_ready")
        relu_done = sem("relu_done")
        exp_done = sem("exp_done")
        stats_ready = sem("stats_ready")
        gate_link = sem("gate_link")
        gate_ready = sem("gate_ready")
        thr_done = sem("thr_done")
        tr_done = sem("tr_done")
        evac_done = sem("evac_done")
        mm_done = sem("mm_done")
        g_ready = sem("g_ready")
        neg_ready = sem("neg_ready")
        eneg_ready = sem("eneg_ready")
        xres_loaded = [sem(f"xres_loaded{i}") for i in range(2)]
        y_link = sem("y_link")
        y_ready = sem("y_ready")
        moments_ready = sem("moments_ready")
        var_ready = sem("var_ready")
        root_link = sem("root_link")
        rs_ready = sem("rs_ready")
        out_ready = sem("out_ready")
        out_stored = [sem(f"out_stored{i}") for i in range(2)]

        block = ctx.enter_context(nc.Block())

        def wait_apart(eng, *waits):
            for semaphore, value in waits:
                eng.wait_ge(semaphore, value)
            eng.sem_inc(passed, 1)

        def slots(eng, slot, last_lag, ahead=0, head=4):
            def straight(k):
                slot(k, k % 2, lambda lag: 0 <= k - lag < NT)

            for k in range(head):
                straight(k)
            with eng.Fori(head // 2, NT // 2 - ahead) as i:
                for u in range(2):
                    slot(i * 2 + u, u, lambda lag: True)
            for k in range(NT - 2 * ahead, NT + last_lag):
                straight(k)

        @block.sync
        def _(sp):
            sp.dma_start(W_sb[:, 0:F], W).then_inc(weights_loaded, 16)
            sp.dma_start(a3[:, 0:1], a[0:F, :]).then_inc(weights_loaded, 16)
            sp.dma_start(a3[:, 1:2], a[F:2 * F, :]).then_inc(weights_loaded, 16)
            for s in range(NXB):
                sp.dma_start(x_in[:, s, :, :], x_steps[s]).then_inc(x_loaded[s], 16)
            with sp.Fori(1, NX // NXB) as i:
                for b in range(NXB):
                    sp.wait_ge(xT_done, i * NXB + (b + 1 - NXB))
                    sp.dma_start(x_in[:, b, :, :], x_steps[bass.ds(i * NXB + b, 1)]
                                 .rearrange("s p t f -> p (s t) f")).then_inc(x_loaded[b], 16)
            for c in range(NCH):
                sp.dma_start(adj_sb[:, c, :], adj_tiles[0, :, c * CH:(c + 1) * CH])\
                  .then_inc(adj_loaded[c], 16)
            sp.wait_ge(qT_copied, 1)
            sp.dma_start(q_dram, qT_sb[:, :]).then_inc(q_stored, 16)
            sp.wait_ge(q_stored, 16)
            for c in range(NCH):
                sp.dma_start(q_row[:, c * CH:(c + 1) * CH],
                             q_flat[c * CH:(c + 1) * CH].partition_broadcast(P))\
                  .then_inc(q_loaded[c], 16)

            def slot(k, u, live):
                v = 1 - u
                for c in range(NCH):
                    if live(0) and not (isinstance(k, int) and k == 0):
                        sp.wait_ge(adj_used, k * NCH + (c + 1 - NCH))
                        sp.dma_start(adj_sb[:, c, :],
                                     adj_tiles[bass.ds(k, 1), :, c * CH:(c + 1) * CH]
                                     .rearrange("t p n -> (t p) n"))\
                          .then_inc(adj_loaded[c], 16)
                    if c == 0 and live(3):
                        if not isinstance(k, int) or k >= 5:
                            sp.wait_ge(y_ready, k - 4)
                        sp.dma_start(x_res[:, v, :], x_tiles[bass.ds(k - 3, 1)]
                                     .rearrange("t p f -> (t p) f")).then_inc(xres_loaded[v], 16)
                    if c == 1 and live(6):
                        sp.wait_ge(out_ready, k - 5)
                        sp.dma_start(out_tiles[bass.ds(k - 6, 1)].rearrange("t p f -> (t p) f"),
                                     o_sb[:, u, :]).then_inc(out_stored[u], 16)

            slots(sp, slot, 6, head=6)
            for u in range(2):
                sp.wait_ge(out_stored[u], 16 * (NT // 2))

        @block.gpsimd
        def _(pool):
            nc.gpsimd.memset(ident[:, :], 0.0).then_inc(consts_zeroed, 1)
            nc.gpsimd.memset(ones[:, :], 1.0).then_inc(consts_ready, 1)
            nc.gpsimd.memset(a3[:, 2:3], 1.0).then_inc(consts_ready, 1)
            for i, value in enumerate((EPS, -EPS / 2, 1.5, float(CH))):
                nc.gpsimd.memset(consts[:, i:i + 1], value).then_inc(consts_ready, 1)
            pool.wait_ge(consts_zeroed, 1)
            nc.gpsimd.affine_select(out=ident[:, :], in_=ident[:, :], compare_op=ALU.not_equal,
                                    fill=1.0, base=0, pattern=[[-1, P]], channel_multiplier=1)\
              .then_inc(consts_ready, 1)

            def slot(k, u, live):
                v = 1 - u
                if live(2):
                    wait_apart(pool, (g_ready, k - 1))
                    nc.gpsimd.tensor_scalar(neg[:, u, :], g_sb[:, u, :], 0.0, 0.0, ALU.min, ALU.add)\
                      .then_inc(neg_ready, 1)
                if live(3):
                    j = k - 3
                    nc.gpsimd.tensor_scalar(elu[:, v, 0, :], g_sb[:, v, :], 0.0, -1.0, ALU.max, ALU.add)\
                      .then_inc(y_link, 1)
                    pool.wait_ge(y_link, j * 2 + 1)
                    pool.wait_ge(eneg_ready, k - 2)
                    nc.gpsimd.tensor_tensor(elu[:, v, 1, :], elu[:, v, 0, :], e_neg[:, v, :], ALU.add)\
                      .then_inc(y_link, 1)
                    pool.wait_ge(y_link, j * 2 + 2)
                    if isinstance(k, int):
                        pool.wait_ge(xres_loaded[v], 16 * (j // 2 + 1))
                    else:
                        pool.wait_ge(xres_loaded[v], (j + (1 if u == 0 else 2)) * 8)
                    nc.gpsimd.tensor_tensor(y_sb[:, v, :], elu[:, v, 1, :], x_res[:, v, :], ALU.add)\
                      .then_inc(y_ready, 1)
                if live(4):
                    j = k - 4
                    if not isinstance(k, int):
                        wait_apart(pool, (rs_ready, k - 3), (out_stored[u], (j - u) * 8))
                    else:
                        pool.wait_ge(rs_ready, k - 3)
                        if j >= 2:
                            pool.wait_ge(out_stored[u], 16 * (j // 2))
                    nc.gpsimd.tensor_scalar(o_sb[:, u, :], y_sb[:, u, :], ln[:, u, 0:1], rs[:, u, 6:7],
                                            ALU.subtract, ALU.mult).then_inc(out_ready, 1)

            slots(pool, slot, 4, head=6)

        @block.scalar
        def _(act):
            nc.scalar.preload_act_table_set("natural_log_exp_and_others")
            act.wait_ge(consts_ready, 7)
            act.wait_ge(WT_done, 1)
            nc.scalar.copy(WT_sb[:, :], w_ps[:, 0:P]).then_inc(WT_copied, 1)
            act.wait_ge(Wa_done, 1)
            nc.scalar.copy(W_sb[:, F:F3], w_ps[:, 128:131]).then_inc(Wa_copied, 1)
            def first(s, u, peeled):
                act.wait_ge(xT_done, s + 1)
                if not peeled:
                    act.wait_ge(first_mm, s - 1)
                nc.scalar.copy(xT[:, u, :], xT_ps[u]).then_inc(xT_copied, 1)
            for s in range(2):
                first(s, s, True)
            with act.Fori(1, NX // 2) as i:
                for u in range(2):
                    first(i * 2 + u, u, False)

            def relu(k, u, c):
                nc.scalar.activation(p_sb[:, u, c * CH:(c + 1) * CH], q_row[:, c * CH:(c + 1) * CH],
                                     ACT.Relu, bias=r_bias[:, bass.ds(k, 1)],
                                     scale=-(1 - ALPHA) / ALPHA).then_inc(relu_done, 1)

            act.wait_ge(bias_ready, 1)
            for c in range(NCH):
                act.wait_ge(q_loaded[c], 16)
                relu(0, 0, c)

            def exp(k, u, c):
                pc = p_sb[:, u, c * CH:(c + 1) * CH]
                nc.scalar.activation(pc, pc, ACT.Exp, bias=shift[:, u:u + 1],
                                     accum_out=sum_c[:, u, c:c + 1]).then_inc(exp_done, 1)

            def evac(k, g):
                n = k * NG + g
                act.wait_ge(tr_done, n + 1)
                if not isinstance(n, int) or n >= NPT:
                    act.wait_ge(mm_done, n + (1 - NPT))
                nc.scalar.copy(pT[:, g % NPT, :], tr_ps[g % NTR][:, :]).then_inc(evac_done, 1)

            def root(u, to, values, function=ACT.Identity, **kw):
                nc.scalar.activation(rs[:, u, to:to + 1], values, function, **kw).then_inc(root_link, 1)

            def stat(u, to, values, **kw):
                nc.scalar.activation(addends[:, u, to, :], values, ACT.Identity,
                                     accum_out=stats[:, u, to:to + 1], **kw).then_inc(stats_ready, 1)

            def sums(k, u):
                act.wait_ge(exp_done, (k + 1) * NCH)
                stat(u, 0, sum_c[:, u, :])
                stat(u, 1, sum_c[:, u, :], scale=THR)
                stat(u, 2, n_inv[:, u, :], scale=-1.0, bias=consts[:, 3:4])

            def slot(k, u, live):
                v = 1 - u
                if live(0):
                    act.wait_ge(rowmax_ready, k + 1)
                    nc.scalar.mul(shift[:, u:u + 1], row_max[:, u:u + 1], -1.0).then_inc(shift_ready, 1)
                    act.wait_ge(shift_ready, k + 1)
                    exp(k, u, 0)
                last = isinstance(k, int) and k == NT - 1
                if last:
                    for c in range(1, NCH):
                        exp(k, u, c)
                    sums(k, u)
                if live(3):
                    act.wait_ge(neg_ready, k - 2)
                    nc.scalar.activation(e_neg[:, v, :], neg[:, v, :], ACT.Exp).then_inc(eneg_ready, 1)
                for c in range(NCH):
                    if live(0) and c + 1 < NCH and not last:
                        exp(k, u, c + 1)
                    if live(1):
                        for g in range(c * GPC, (c + 1) * GPC):
                            evac(k - 1, g)
                    if live(-1):
                        relu(k + 1, v, c)
                    if c == 1 and live(4):
                        act.wait_ge(var_ready, k - 3)
                        root(u, 0, ln[:, u, 1:2], bias=consts[:, 0:1])
                        root(u, 1, ln[:, u, 1:2], scale=-0.5, bias=consts[:, 1:2])
                    if c == 2 and live(4):
                        act.wait_ge(root_link, (k - 4) * 6 + 1)
                        root(u, 2, rs[:, u, 0:1], ACT.Ln)
                    if c == 3 and live(4):
                        act.wait_ge(root_link, (k - 4) * 6 + 3)
                        root(u, 3, rs[:, u, 2:3], ACT.Exp, scale=-0.5)
                if live(0) and not last:
                    sums(k, u)
                if live(4):
                    act.wait_ge(root_link, (k - 4) * 6 + 4)
                    root(u, 4, rs[:, u, 3:4], scale=rs[:, u, 3:4])
                    act.wait_ge(root_link, (k - 4) * 6 + 5)
                    root(u, 5, rs[:, u, 4:5], scale=rs[:, u, 1:2], bias=consts[:, 2:3])
                    act.wait_ge(root_link, (k - 3) * 6)
                    nc.scalar.activation(rs[:, u, 6:7], rs[:, u, 5:6], ACT.Identity,
                                         scale=rs[:, u, 3:4]).then_inc(rs_ready, 1)

            slots(act, slot, 4, ahead=1)

        @block.vector
        def _(dve):
            def first(s, u):
                dve.wait_ge(first_mm, s + 1)
                for half in range(2):
                    nc.vector.tensor_copy(h_sb[:, bass.ds(s * XB + half * 2, 2), :],
                                          hs_ps[u][half].rearrange("p (t f) -> p t f", t=2))\
                      .then_inc(h_copied, 1)
            with dve.Fori(0, NX // 2) as i:
                for u in range(2):
                    first(i * 2 + u, u)
            dve.wait_ge(h_copied, NX * 2)
            nc.vector.tensor_reduce(d_max[:, 0:1], d_col,
                                    AX.X, ALU.max).then_inc(dmax_done, 1)
            dve.wait_ge(dmaxT_done, 1)
            nc.vector.tensor_reduce(d_max[0:1, 1:2], k_ps[0:1, 0:P], AX.X, ALU.max).then_inc(dtop_done, 1)
            dve.wait_ge(dtop_spread, 1)
            nc.vector.tensor_scalar(K_sb[:, 0:1], k_ps[:, P:P + 1], ALPHA / BIG, None, ALU.mult)\
              .then_inc(K_ready, 1)
            nc.vector.tensor_scalar(K_sb[:, 1:2], k_ps[:, P:P + 1], (1 - ALPHA) / BIG, None, ALU.mult)\
              .then_inc(K_ready, 1)
            dve.wait_ge(K_ready, 2)
            nc.vector.tensor_scalar(q_col[:, :], d_col,
                                    -ALPHA / BIG, K_sb[:, 0:1], ALU.mult, ALU.add).then_inc(q_link, 1)
            dve.wait_ge(q_link, 1)
            nc.vector.scalar_tensor_tensor(out=q_col[:, :],
                                           in0=sum_col,
                                           scalar=0.0, in1=q_col[:, :],
                                           op0=ALU.is_equal, op1=ALU.max).then_inc(q_link, 1)
            nc.vector.tensor_scalar(r_bias[:, :], s_col,
                                    (1 - ALPHA) / BIG, K_sb[:, 1:2], ALU.mult, ALU.add)\
              .then_inc(bias_ready, 1)
            dve.wait_ge(qT_done, 1)
            nc.vector.tensor_copy(qT_sb[:, :], k_ps[0:NT, 2 * P:3 * P]).then_inc(qT_copied, 1)

            def slot(k, u, live):
                v = 1 - u
                def w_pass(c):
                    dve.wait_ge(adj_loaded[c], (k + 1) * 16)
                    if isinstance(k, int) and k == 0:
                        dve.wait_ge(q_loaded[c], 16)
                    if c >= 2:
                        wait_apart(dve, (masked_ready, k * NCH + (c - 1)))
                    nc.vector.scalar_tensor_tensor(
                        out=w_sb[:, c % 2, :], in0=adj_sb[:, c, :], scalar=0.0,
                        in1=q_row[:, c * CH:(c + 1) * CH], op0=ALU.is_le, op1=ALU.max,
                        accum_out=n_inv[:, u, c:c + 1]).then_inc(adj_used, 1)

                def logits(c):
                    cols = slice(c * CH, (c + 1) * CH)
                    wait_apart(dve, (adj_used, k * NCH + (c + 1)), (relu_done, k * NCH + (c + 1)))
                    nc.vector.tensor_tensor_reduce(
                        out=p_sb[:, u, cols], in0=p_sb[:, u, cols], in1=w_sb[:, c % 2, :],
                        scale=BIG, scalar=-4.0 * BIG, op0=ALU.subtract, op1=ALU.max,
                        accum_out=max_c[:, u, c:c + 1]).then_inc(masked_ready, 1)

                if live(0):
                    for c in range(0, NCH, 2):
                        w_pass(c)
                        w_pass(c + 1)
                        logits(c)
                        logits(c + 1)
                if live(4):
                    dve.wait_ge(y_ready, k - 3)
                    nc.vector.bn_stats(moments[:, u, :], y_sb[:, u, :]).then_inc(moments_ready, 1)
                if live(0):
                    dve.wait_ge(masked_ready, (k + 1) * NCH)
                    nc.vector.tensor_reduce(row_max[:, u:u + 1], max_c[:, u, :], AX.X, ALU.max)\
                      .then_inc(rowmax_ready, 1)
                if live(1):
                    dve.wait_ge(stats_ready, k * 3)
                    nc.vector.reciprocal(gate[:, v, 0:1], stats[:, v, 0:1]).then_inc(gate_link, 1)
                    for c in range(NCH):
                        pc = p_sb[:, v, c * CH:(c + 1) * CH]
                        nc.vector.scalar_tensor_tensor(out=pc, in0=pc, scalar=stats[:, v, 1:2], in1=pc,
                                                       op0=ALU.is_ge, op1=ALU.mult).then_inc(thr_done, 1)
                        if c == 0:
                            dve.wait_ge(gate_link, k * 2 - 1)
                            nc.vector.scalar_tensor_tensor(
                                out=gate[:, v, 1:2], in0=gate[:, v, 0:1], scalar=THR,
                                in1=stats[:, v, 2:3], op0=ALU.is_gt, op1=ALU.mult).then_inc(gate_link, 1)
                        if c == 1:
                            dve.wait_ge(gate_link, k * 2)
                            nc.vector.tensor_tensor(gate[:, v, 2:3], gate[:, v, 1:2], gate[:, v, 0:1],
                                                    ALU.mult).then_inc(gate_ready, 1)
                if live(4):
                    wait_apart(dve, (moments_ready, k - 3))
                    nc.vector.bn_aggr(ln[:, u, 0:2], moments[:, u, :]).then_inc(var_ready, 1)
                if live(2):
                    dve.wait_ge(mm_done, (k - 1) * NG)
                    dve.wait_ge(gate_ready, k - 1)
                    if not isinstance(k, int) or k >= 4:
                        dve.wait_ge(y_ready, k - 3)
                    nc.vector.scalar_tensor_tensor(
                        out=g_sb[:, u, :], in0=acc_ps[u][:, 0:F], scalar=gate[:, u, 2:3],
                        in1=h_sb[:, bass.ds(k - 2, 1), 0:F].rearrange("p a f -> p (a f)"),
                        op0=ALU.mult, op1=ALU.add).then_inc(g_ready, 1)

            slots(dve, slot, 4)

        @block.tensor
        def _(pe):
            pe.wait_ge(consts_ready, 7)
            pe.wait_ge(weights_loaded, 48)
            nc.tensor.transpose(w_ps[:, 0:P], W_sb[:, 0:F], ident[:, :]).then_inc(WT_done, 1)
            pe.wait_ge(WT_copied, 1)
            nc.tensor.matmul(w_ps[:, 128:131], WT_sb[:, :], a3[:, :], start=True, stop=True)\
              .then_inc(Wa_done, 1)
            pe.wait_ge(Wa_copied, 1)

            def first(s, b, loads):
                u = b % 2
                pe.wait_ge(x_loaded[b], loads * 16)
                if not isinstance(s, int) or s >= 2:
                    pe.wait_ge(xT_copied, s - 1)
                for t in range(XB):
                    last = nc.tensor.transpose(xT_ps[u][:, t * P:(t + 1) * P],
                                               x_in[:, b, t, :], ident[:, :])
                last.then_inc(xT_done, 1)
                if not isinstance(s, int) or s >= 1:
                    pe.wait_ge(xT_copied, s)
                    if not isinstance(s, int) or s >= 3:
                        pe.wait_ge(h_copied, (s - 2) * 2)
                    products_of_x(1 - u)

            def products_of_x(u):
                for t in range(XB):
                    last = nc.tensor.matmul(hs_ps[u][t // 2][:, (t % 2) * F3:(t % 2 + 1) * F3],
                                            xT[:, u, t * P:(t + 1) * P], W_sb[:, :],
                                            start=True, stop=True)
                last.then_inc(first_mm, 1)

            for s in range(NXB):
                first(s, s, 1)
            with pe.Fori(1, NX // NXB) as i:
                for b in range(NXB):
                    first(i * NXB + b, b, i + 1)
            pe.wait_ge(xT_copied, NX)
            pe.wait_ge(h_copied, (NX - 2) * 2)
            products_of_x((NX - 1) % 2)
            pe.wait_ge(dmax_done, 1)
            nc.tensor.transpose(k_ps[0:1, 0:P], d_max[:, 0:1], ident[:, :]).then_inc(dmaxT_done, 1)
            pe.wait_ge(dtop_done, 1)
            nc.tensor.matmul(k_ps[:, P:P + 1], ones[:, :], d_max[0:1, 1:2], start=True, stop=True)\
              .then_inc(dtop_spread, 1)
            pe.wait_ge(q_link, 2)
            nc.tensor.transpose(k_ps[0:NT, 2 * P:3 * P], q_col[:, :], ident[:, :]).then_inc(qT_done, 1)

            def tile(k, u, peeled):
                def transposes(g):
                    n = k * NG + g
                    if g % GPC == 0:
                        pe.wait_ge(thr_done, k * NCH + (g // GPC + 1))
                    if not peeled or n >= NTR:
                        pe.wait_ge(evac_done, n + (1 - NTR))
                    for b in range(GB):
                        at = g * GC + b * P
                        last = nc.tensor.transpose(tr_ps[g % NTR][:, b * P:(b + 1) * P],
                                                   p_sb[:, u, at:at + P], ident[:, :])
                    last.then_inc(tr_done, 1)

                def products(g):
                    pe.wait_ge(evac_done, k * NG + (g + 1))
                    if g == 0 and (not peeled or k >= 2):
                        pe.wait_ge(g_ready, k - 1)
                    for b in range(GB):
                        j = g * GB + b
                        last = nc.tensor.matmul(acc_ps[u][:, 0:F], pT[:, g % NPT, b * P:(b + 1) * P],
                                                h_sb[:, j, 0:F], start=(j == 0), stop=(j == NT - 1))
                    last.then_inc(mm_done, 1)

                for g in range(NG + AHEAD):
                    if g < NG:
                        transposes(g)
                    if g >= AHEAD:
                        products(g - AHEAD)

            for k in range(2):
                tile(k, k, True)
            with pe.Fori(1, NT // 2) as i:
                for u in range(2):
                    tile(i * 2 + u, u, False)


_INS = ["x", "adj", "L0_gnn_W", "L0_gnn_a"]


def kernel(**inputs):
    import numpy as _np
    import concourse.bacc as _bacc
    from concourse import mybir as _mybir
    from concourse.bass_utils import run_bass_kernel_spmd as _run

    nc = _bacc.Bacc("TRN2", target_bir_lowering=False, num_devices=1)
    arrays, args = {}, []
    for name in _INS:
        array = _np.ascontiguousarray(inputs[name])
        arrays[f"in_{name}"] = array
        args.append(nc.dram_tensor(f"in_{name}", array.shape, _mybir.dt.from_np(array.dtype),
                                   kind="ExternalInput").ap())
    shape = inputs["x"].shape
    q_dram = nc.dram_tensor("q_dram", (shape[0] // 128, 128), _mybir.dt.float32).ap()
    out = nc.dram_tensor("out_dram", shape, _mybir.dt.float32, kind="ExternalOutput").ap()
    graph_attention_layer(nc, *args, q_dram, out)
    r = _run(nc, [arrays], core_ids=[0])
    return r.results[0]["out_dram"]
```

```python
import concourse.bass as bass
from concourse import mybir
from contextlib import ExitStack


def graph_attention_layer(nc, x, adj, W, a, q_dram, out):
    fp32, i32 = mybir.dt.float32, mybir.dt.int32
    ALU = mybir.AluOpType
    ACT = mybir.ActivationFunctionType
    AX = mybir.AxisListType

    N, F = x.shape
    P = 128
    F3 = F + 3
    NT = N // P
    CH = 4096
    NCH = N // CH
    TC = 2048
    NTC = N // TC
    GB = 8
    GC = GB * P
    NG = N // GC
    GPT = TC // GC
    HG = CH // GC
    NTR = 2
    NPT = 4
    XB = 4
    XC = XB * P
    NX = NT // XB
    NXB = 4
    ALPHA, THR, EPS = 0.2, 1e-4, 1e-5
    BIG = float(2 ** 60)

    x_tiles = x.rearrange("(t p) f -> t p f", p=P)
    x_steps = x.rearrange("(s t p) f -> s p t f", t=XB, p=P)
    q_flat = q_dram.rearrange("t p -> (t p)")
    adj_tiles = adj.rearrange("(t p) n -> t p n", p=P)
    out_tiles = out.rearrange("(t p) f -> t p f", p=P)

    ctx = ExitStack()
    with ctx:
        def sb(name, shape, dt=fp32):
            return ctx.enter_context(nc.sbuf_tensor(name, shape, dt))

        def sem(name):
            return ctx.enter_context(nc.semaphore(name))

        ident = sb("ident", [P, P])
        ones = sb("ones", [1, P])
        W_sb = sb("W_sb", [P, F3])
        WT_sb = sb("WT_sb", [P, P])
        a3 = sb("a3", [P, 3])
        h_sb = sb("h_sb", [P, NT, F3])
        s_col, d_col, sum_col = (h_sb[:, :, F + i:F + i + 1].rearrange("p t a -> p (t a)")
                                 for i in range(3))
        q_row = sb("q_row", [P, N])
        adj_sb = sb("adj_sb", [P, NCH, CH], i32)
        w_sb = sb("w_sb", [P, CH])
        p_sb = sb("p_sb", [P, 2, N])
        pT = sb("pT", [P, NPT, GC])
        xT = pT[:, 0, :].rearrange("p (s c) -> p s c", s=2)
        x_in = p_sb[:, 1, 0:NXB * XC].rearrange("p (s t f) -> p s t f", s=NXB, t=XB)
        n_inv = sb("n_inv", [P, 2, NCH])
        n_part = sb("n_part", [P, 2])
        d_max = sb("d_max", [P, 2])
        K_sb = sb("K_sb", [P, 2])
        q_col = sb("q_col", [P, NT])
        qT_sb = sb("qT_sb", [NT, P])
        r_bias = sb("r_bias", [P, NT])
        max_c = sb("max_c", [P, 2, NCH])
        row_max = sb("row_max", [P, 2])
        shift = sb("shift", [P, 2])
        sum_c = sb("sum_c", [P, 2, NCH])
        stats = sb("stats", [P, 2, 3])
        addends = sb("addends", [P, 2, 3, NCH])
        gate = sb("gate", [P, 2, 3])
        hp_sb = sb("hp_sb", [P, 2, F])
        g_sb = sb("g_sb", [P, 2, F])
        neg = sb("neg", [P, 2, F])
        e_neg = sb("e_neg", [P, 2, F])
        x_res = sb("x_res", [P, 2, F])
        y_sb = sb("y_sb", [P, 2, F])
        pos = sb("pos", [P, 2, F])
        elu = sb("elu", [P, 2, F])
        spread = sb("spread", [P, 2, 2, F])
        consts = sb("consts", [P, 5])
        rs = sb("rs", [P, 2, 10])
        o_sb = sb("o_sb", [P, 2, F])

        tr_ps = [ctx.enter_context(nc.psum_tensor(f"tr_ps{i}", [P, GC], fp32)) for i in range(NTR)]
        acc_ps = [ctx.enter_context(nc.psum_tensor(f"acc_ps{i}", [P, 512], fp32)) for i in range(2)]
        h_ps = [ctx.enter_context(nc.psum_tensor(f"h_ps{i}", [P, 512], fp32)) for i in range(2)]
        xT_ps = [tr_ps[i][:, 0:512] for i in range(2)]
        hs_ps = [[h_ps[i][:, 0:2 * F3], tr_ps[i][:, 512:512 + 2 * F3]] for i in range(2)]
        k_ps = acc_ps[1]
        w_ps = acc_ps[0]

        passed = sem("passed")
        consts_zeroed = sem("consts_zeroed")
        consts_ready = sem("consts_ready")
        weights_loaded = sem("weights_loaded")
        WT_done = sem("WT_done")
        WT_copied = sem("WT_copied")
        Wa_done = sem("Wa_done")
        Wa_copied = sem("Wa_copied")
        x_loaded = [sem(f"x_loaded{i}") for i in range(NXB)]
        xT_done = sem("xT_done")
        xT_copied = sem("xT_copied")
        first_mm = sem("first_mm")
        h_copied = sem("h_copied")
        adj_loaded = [sem(f"adj_loaded{c}") for c in range(NCH)]
        adj_used = sem("adj_used")
        w_link = sem("w_link")
        masked_ready = sem("masked_ready")
        rowmax_ready = sem("rowmax_ready")
        dmax_done = sem("dmax_done")
        dmaxT_done = sem("dmaxT_done")
        dtop_done = sem("dtop_done")
        dtop_spread = sem("dtop_spread")
        K_ready = sem("K_ready")
        q_link = sem("q_link")
        qT_done = sem("qT_done")
        qT_copied = sem("qT_copied")
        q_stored = sem("q_stored")
        q_loaded = [sem(f"q_loaded{c}") for c in range(NTC)]
        bias_ready = sem("bias_ready")
        shift_ready = sem("shift_ready")
        relu_done = sem("relu_done")
        exp_done = sem("exp_done")
        stats_ready = sem("stats_ready")
        gate_link = sem("gate_link")
        gate_ready = sem("gate_ready")
        thr_done = sem("thr_done")
        tr_done = sem("tr_done")
        evac_done = sem("evac_done")
        mm_done = sem("mm_done")
        g_ready = sem("g_ready")
        hp_ready = sem("hp_ready")
        neg_ready = sem("neg_ready")
        recip_ready = sem("recip_ready")
        eneg_ready = sem("eneg_ready")
        xres_loaded = [sem(f"xres_loaded{i}") for i in range(2)]
        y_link = sem("y_link")
        y_ready = sem("y_ready")
        root_link = sem("root_link")
        rs_ready = sem("rs_ready")
        out_ready = sem("out_ready")
        out_stored = [sem(f"out_stored{i}") for i in range(2)]

        block = ctx.enter_context(nc.Block())

        def wait_apart(eng, *waits):
            for semaphore, value in waits:
                eng.wait_ge(semaphore, value)
            eng.sem_inc(passed, 1)

        def slots(eng, slot, last_lag, ahead=0, head=4):
            def straight(k):
                slot(k, k % 2, lambda lag: 0 <= k - lag < NT)

            for k in range(head):
                straight(k)
            with eng.Fori(head // 2, NT // 2 - ahead) as i:
                for u in range(2):
                    slot(i * 2 + u, u, lambda lag: True)
            for k in range(NT - 2 * ahead, NT + last_lag):
                straight(k)

        @block.sync
        def _(sp):
            sp.dma_start(W_sb[:, 0:F], W).then_inc(weights_loaded, 16)
            sp.dma_start(a3[:, 0:1], a[0:F, :]).then_inc(weights_loaded, 16)
            sp.dma_start(a3[:, 1:2], a[F:2 * F, :]).then_inc(weights_loaded, 16)
            for s in range(NXB):
                sp.dma_start(x_in[:, s, :, :], x_steps[s]).then_inc(x_loaded[s], 16)
            with sp.Fori(1, NX // NXB) as i:
                for b in range(NXB):
                    sp.wait_ge(xT_done, i * NXB + (b + 1 - NXB))
                    sp.dma_start(x_in[:, b, :, :], x_steps[bass.ds(i * NXB + b, 1)]
                                 .rearrange("s p t f -> p (s t) f")).then_inc(x_loaded[b], 16)
            for c in range(NCH):
                sp.dma_start(adj_sb[:, c, :], adj_tiles[0, :, c * CH:(c + 1) * CH])\
                  .then_inc(adj_loaded[c], 16)
            sp.wait_ge(qT_copied, 1)
            sp.dma_start(q_dram, qT_sb[:, :]).then_inc(q_stored, 16)
            sp.wait_ge(q_stored, 16)
            for c in range(NTC):
                sp.dma_start(q_row[:, c * TC:(c + 1) * TC],
                             q_flat[c * TC:(c + 1) * TC].partition_broadcast(P))\
                  .then_inc(q_loaded[c], 16)

            def slot(k, u, live):
                v = 1 - u
                for c in range(NCH):
                    if live(0) and not (isinstance(k, int) and k == 0):
                        sp.wait_ge(adj_used, k * NCH + (c + 1 - NCH))
                        sp.dma_start(adj_sb[:, c, :],
                                     adj_tiles[bass.ds(k, 1), :, c * CH:(c + 1) * CH]
                                     .rearrange("t p n -> (t p) n"))\
                          .then_inc(adj_loaded[c], 16)
                    if c == 0 and live(3):
                        if not isinstance(k, int) or k >= 5:
                            sp.wait_ge(y_ready, k - 4)
                        sp.dma_start(x_res[:, v, :], x_tiles[bass.ds(k - 3, 1)]
                                     .rearrange("t p f -> (t p) f")).then_inc(xres_loaded[v], 16)
                    if c == 1 and live(6):
                        sp.wait_ge(out_ready, k - 5)
                        sp.dma_start(out_tiles[bass.ds(k - 6, 1)].rearrange("t p f -> (t p) f"),
                                     o_sb[:, u, :]).then_inc(out_stored[u], 16)

            slots(sp, slot, 6, head=6)
            for u in range(2):
                sp.wait_ge(out_stored[u], 16 * (NT // 2))

        @block.gpsimd
        def _(pool):
            nc.gpsimd.memset(ident[:, :], 0.0).then_inc(consts_zeroed, 1)
            nc.gpsimd.memset(ones[:, :], 1.0).then_inc(consts_ready, 1)
            nc.gpsimd.memset(a3[:, 2:3], 1.0).then_inc(consts_ready, 1)
            for i, value in enumerate((EPS, -EPS / 2, 1.5, float(CH), -1.0)):
                nc.gpsimd.memset(consts[:, i:i + 1], value).then_inc(consts_ready, 1)
            pool.wait_ge(consts_zeroed, 1)
            nc.gpsimd.affine_select(out=ident[:, :], in_=ident[:, :], compare_op=ALU.not_equal,
                                    fill=1.0, base=0, pattern=[[-1, P]], channel_multiplier=1)\
              .then_inc(consts_ready, 1)

            def slot(k, u, live):
                v = 1 - u
                if live(1):
                    wait_apart(pool, (recip_ready, k))
                    nc.gpsimd.tensor_scalar(gate[:, v, 1:2], gate[:, v, 0:1], THR, stats[:, v, 2:3],
                                            ALU.is_gt, ALU.mult).then_inc(gate_link, 1)
                if live(2):
                    pool.wait_ge(hp_ready, k - 1)
                    nc.gpsimd.tensor_tensor(g_sb[:, u, :], hp_sb[:, u, :],
                                            h_sb[:, bass.ds(k - 2, 1), 0:F].rearrange("p a f -> p (a f)"),
                                            ALU.add).then_inc(g_ready, 1)
                if live(3):
                    j = k - 3
                    pool.wait_ge(eneg_ready, (k - 2) * 2)
                    nc.gpsimd.tensor_tensor(elu[:, v, :], pos[:, v, :], e_neg[:, v, :], ALU.add)\
                      .then_inc(y_link, 1)
                    pool.wait_ge(y_link, k - 2)
                    if isinstance(k, int):
                        pool.wait_ge(xres_loaded[v], 16 * (j // 2 + 1))
                    else:
                        pool.wait_ge(xres_loaded[v], (j + (1 if u == 0 else 2)) * 8)
                    nc.gpsimd.tensor_tensor(y_sb[:, v, :], elu[:, v, :], x_res[:, v, :], ALU.add)\
                      .then_inc(y_ready, 1)
                if live(4):
                    j = k - 4
                    if not isinstance(k, int):
                        wait_apart(pool, (rs_ready, k - 3), (out_stored[u], (j - u) * 8))
                    else:
                        pool.wait_ge(rs_ready, k - 3)
                        if j >= 2:
                            pool.wait_ge(out_stored[u], 16 * (j // 2))
                    nc.gpsimd.tensor_scalar(o_sb[:, u, :], y_sb[:, u, :], rs[:, u, 1:2], rs[:, u, 9:10],
                                            ALU.add, ALU.mult).then_inc(out_ready, 1)

            slots(pool, slot, 4, head=6)

        @block.scalar
        def _(act):
            nc.scalar.preload_act_table_set("natural_log_exp_and_others")
            act.wait_ge(consts_ready, 8)
            act.wait_ge(WT_done, 1)
            nc.scalar.copy(WT_sb[:, :], w_ps[:, 0:P]).then_inc(WT_copied, 1)
            act.wait_ge(Wa_done, 1)
            nc.scalar.copy(W_sb[:, F:F3], w_ps[:, P:P + 3]).then_inc(Wa_copied, 1)
            def first(s, u, peeled):
                act.wait_ge(xT_done, s + 1)
                if not peeled:
                    act.wait_ge(first_mm, s - 1)
                nc.scalar.copy(xT[:, u, :], xT_ps[u]).then_inc(xT_copied, 1)
            for s in range(2):
                first(s, s, True)
            with act.Fori(1, NX // 2) as i:
                for u in range(2):
                    first(i * 2 + u, u, False)

            def relu(k, u, first, last):
                nc.scalar.activation(p_sb[:, u, first:last], q_row[:, first:last],
                                     ACT.Relu, bias=r_bias[:, bass.ds(k, 1)],
                                     scale=-(1 - ALPHA) / ALPHA).then_inc(relu_done, 1)

            act.wait_ge(bias_ready, 1)
            act.wait_ge(q_loaded[0], 16)
            relu(0, 0, 0, TC)
            act.wait_ge(q_loaded[1], 16)
            relu(0, 0, TC, CH)
            act.wait_ge(q_loaded[2], 16)
            act.wait_ge(q_loaded[3], 16)
            relu(0, 0, CH, N)
            relu(1, 1, 0, TC)
            relu(1, 1, TC, CH)

            def exp(k, u, c):
                pc = p_sb[:, u, c * CH:(c + 1) * CH]
                nc.scalar.activation(pc, pc, ACT.Exp, bias=shift[:, u:u + 1],
                                     accum_out=sum_c[:, u, c:c + 1]).then_inc(exp_done, 1)

            def evac(k, g):
                n = k * NG + g
                act.wait_ge(tr_done, n + 1)
                if not isinstance(n, int) or n >= NPT:
                    act.wait_ge(mm_done, n + (1 - NPT))
                nc.scalar.copy(pT[:, g % NPT, :], tr_ps[g % NTR][:, :]).then_inc(evac_done, 1)

            def root(u, to, values, function=ACT.Identity, **kw):
                nc.scalar.activation(rs[:, u, to:to + 1], values, function, **kw).then_inc(root_link, 1)

            def stat(u, to, values, **kw):
                nc.scalar.activation(addends[:, u, to, :], values, ACT.Identity,
                                     accum_out=stats[:, u, to:to + 1], **kw).then_inc(stats_ready, 1)

            def slot(k, u, live):
                v = 1 - u
                if live(0):
                    act.wait_ge(rowmax_ready, k + 1)
                    nc.scalar.mul(shift[:, u:u + 1], row_max[:, u:u + 1], -1.0).then_inc(shift_ready, 1)
                    act.wait_ge(shift_ready, k + 1)
                    exp(k, u, 0)
                if live(2):
                    act.wait_ge(gate_link, k - 1)
                    nc.scalar.activation(gate[:, u, 2:3], gate[:, u, 1:2], ACT.Identity,
                                         scale=gate[:, u, 0:1]).then_inc(gate_ready, 1)
                if live(1):
                    evac(k - 1, HG)
                    evac(k - 1, HG + 1)
                if live(0):
                    exp(k, u, 1)
                if live(2):
                    act.wait_ge(mm_done, (k - 1) * NG)
                    act.wait_ge(gate_ready, k - 1)
                    nc.scalar.activation(hp_sb[:, u, :], acc_ps[u][:, 0:F], ACT.Identity,
                                         scale=gate[:, u, 2:3]).then_inc(hp_ready, 1)
                if live(0):
                    act.wait_ge(exp_done, (k + 1) * NCH)
                    stat(u, 0, sum_c[:, u, :])
                    stat(u, 1, sum_c[:, u, :], scale=THR)
                    stat(u, 2, n_inv[:, u, :], scale=-1.0, bias=consts[:, 3:4])
                if live(3):
                    act.wait_ge(g_ready, k - 2)
                    nc.scalar.activation(neg[:, v, :], g_sb[:, v, :], ACT.Relu, scale=-1.0)\
                      .then_inc(neg_ready, 1)
                if live(1):
                    evac(k - 1, HG + 2)
                    evac(k - 1, HG + 3)
                if live(3):
                    act.wait_ge(neg_ready, k - 2)
                    nc.scalar.activation(e_neg[:, v, :], neg[:, v, :], ACT.Exp, scale=-1.0)\
                      .then_inc(eneg_ready, 1)
                    nc.scalar.activation(pos[:, v, :], g_sb[:, v, :], ACT.Relu)\
                      .then_inc(eneg_ready, 1)
                if live(-1):
                    relu(k + 1, v, CH, N)
                if live(4):
                    act.wait_ge(y_ready, k - 3)
                    nc.scalar.activation(spread[:, u, 0, :], y_sb[:, u, :], ACT.Identity,
                                         bias=consts[:, 4:5], accum_out=rs[:, u, 0:1]).then_inc(root_link, 1)
                if live(0):
                    evac(k, 0)
                if live(4):
                    act.wait_ge(root_link, (k - 4) * 9 + 1)
                    root(u, 1, rs[:, u, 0:1], scale=-1.0 / F, bias=consts[:, 4:5])
                if live(0):
                    evac(k, 1)
                if live(4):
                    act.wait_ge(root_link, (k - 4) * 9 + 2)
                    nc.scalar.activation(spread[:, u, 1, :], y_sb[:, u, :], ACT.Square,
                                         bias=rs[:, u, 1:2], accum_out=rs[:, u, 2:3])\
                      .then_inc(root_link, 1)
                if live(-2):
                    relu(k + 2, u, 0, TC)
                if live(4):
                    act.wait_ge(root_link, (k - 4) * 9 + 3)
                    root(u, 3, rs[:, u, 2:3], scale=1.0 / F, bias=consts[:, 0:1])
                    root(u, 4, rs[:, u, 2:3], scale=-0.5 / F, bias=consts[:, 1:2])
                    act.wait_ge(root_link, (k - 4) * 9 + 4)
                    root(u, 5, rs[:, u, 3:4], ACT.Ln)
                if live(0):
                    evac(k, 2)
                if live(4):
                    act.wait_ge(root_link, (k - 4) * 9 + 6)
                    root(u, 6, rs[:, u, 5:6], ACT.Exp, scale=-0.5)
                if live(0):
                    evac(k, 3)
                if live(4):
                    act.wait_ge(root_link, (k - 4) * 9 + 7)
                    root(u, 7, rs[:, u, 6:7], scale=rs[:, u, 6:7])
                if live(-2):
                    relu(k + 2, u, TC, CH)
                if live(4):
                    act.wait_ge(root_link, (k - 4) * 9 + 8)
                    root(u, 8, rs[:, u, 7:8], scale=rs[:, u, 4:5], bias=consts[:, 2:3])
                    act.wait_ge(root_link, (k - 3) * 9)
                    nc.scalar.activation(rs[:, u, 9:10], rs[:, u, 8:9], ACT.Identity,
                                         scale=rs[:, u, 6:7]).then_inc(rs_ready, 1)

            slots(act, slot, 4, ahead=1)

        @block.vector
        def _(dve):
            def first(s, u):
                dve.wait_ge(first_mm, s + 1)
                for half in range(2):
                    nc.vector.tensor_copy(h_sb[:, bass.ds(s * XB + half * 2, 2), :],
                                          hs_ps[u][half].rearrange("p (t f) -> p t f", t=2))\
                      .then_inc(h_copied, 1)
            with dve.Fori(0, NX // 2) as i:
                for u in range(2):
                    first(i * 2 + u, u)
            dve.wait_ge(h_copied, NX * 2)
            nc.vector.tensor_reduce(d_max[:, 0:1], d_col, AX.X, ALU.max).then_inc(dmax_done, 1)
            dve.wait_ge(dmaxT_done, 1)
            nc.vector.tensor_reduce(d_max[0:1, 1:2], k_ps[0:1, 0:P], AX.X, ALU.max).then_inc(dtop_done, 1)
            dve.wait_ge(dtop_spread, 1)
            nc.vector.tensor_scalar(K_sb[:, 0:1], k_ps[:, P:P + 1], ALPHA / BIG, None, ALU.mult)\
              .then_inc(K_ready, 1)
            nc.vector.tensor_scalar(K_sb[:, 1:2], k_ps[:, P:P + 1], (1 - ALPHA) / BIG, None, ALU.mult)\
              .then_inc(K_ready, 1)
            dve.wait_ge(K_ready, 2)
            nc.vector.tensor_scalar(q_col[:, :], d_col,
                                    -ALPHA / BIG, K_sb[:, 0:1], ALU.mult, ALU.add).then_inc(q_link, 1)
            dve.wait_ge(q_link, 1)
            nc.vector.scalar_tensor_tensor(out=q_col[:, :], in0=sum_col, scalar=0.0, in1=q_col[:, :],
                                           op0=ALU.is_equal, op1=ALU.max).then_inc(q_link, 1)
            nc.vector.tensor_scalar(r_bias[:, :], s_col,
                                    (1 - ALPHA) / BIG, K_sb[:, 1:2], ALU.mult, ALU.add)\
              .then_inc(bias_ready, 1)
            dve.wait_ge(qT_done, 1)
            nc.vector.tensor_copy(qT_sb[:, :], k_ps[0:NT, 2 * P:3 * P]).then_inc(qT_copied, 1)

            def slot(k, u, live):
                v = 1 - u

                def w_pass(c):
                    dve.wait_ge(adj_loaded[c], (k + 1) * 16)
                    if c >= 1:
                        wait_apart(dve, (masked_ready, k * NCH + c))
                    if isinstance(k, int) and k == 0 and c == 0:
                        for i in range(2):
                            dve.wait_ge(q_loaded[i], 16)
                            masks(c, i * TC, (i + 1) * TC, n_part[:, i:i + 1], w_link)
                        dve.wait_ge(w_link, 2)
                        nc.vector.tensor_tensor(n_inv[:, u, 0:1], n_part[:, 0:1], n_part[:, 1:2],
                                                ALU.add).then_inc(adj_used, 1)
                    else:
                        if isinstance(k, int) and k == 0:
                            dve.wait_ge(q_loaded[2], 16)
                            dve.wait_ge(q_loaded[3], 16)
                        masks(c, 0, CH, n_inv[:, u, c:c + 1], adj_used)

                def masks(c, first, last, count, done):
                    nc.vector.scalar_tensor_tensor(
                        out=w_sb[:, first:last], in0=adj_sb[:, c, first:last], scalar=0.0,
                        in1=q_row[:, c * CH + first:c * CH + last], op0=ALU.is_le, op1=ALU.max,
                        accum_out=count).then_inc(done, 1)

                def logits(c):
                    cols = slice(c * CH, (c + 1) * CH)
                    wait_apart(dve, (adj_used, k * NCH + (c + 1)), (relu_done, k * 3 + (c + 2)))
                    nc.vector.tensor_tensor_reduce(
                        out=p_sb[:, u, cols], in0=p_sb[:, u, cols], in1=w_sb[:, :],
                        scale=BIG, scalar=-4.0 * BIG, op0=ALU.subtract, op1=ALU.max,
                        accum_out=max_c[:, u, c:c + 1]).then_inc(masked_ready, 1)

                def threshold(tile_parity, c):
                    pc = p_sb[:, tile_parity, c * TC:(c + 1) * TC]
                    nc.vector.scalar_tensor_tensor(out=pc, in0=pc, scalar=stats[:, tile_parity, 1:2],
                                                   in1=pc, op0=ALU.is_ge, op1=ALU.mult)\
                      .then_inc(thr_done, 1)

                if live(0):
                    w_pass(0)
                if live(2):
                    threshold(u, 3)
                if live(0):
                    logits(0)
                if live(1):
                    dve.wait_ge(stats_ready, k * 3)
                    threshold(v, 0)
                if live(0):
                    w_pass(1)
                if live(1):
                    threshold(v, 1)
                if live(0):
                    logits(1)
                if live(1):
                    nc.vector.reciprocal(gate[:, v, 0:1], stats[:, v, 0:1]).then_inc(recip_ready, 1)
                if live(0):
                    dve.wait_ge(masked_ready, (k + 1) * NCH)
                    nc.vector.tensor_reduce(row_max[:, u:u + 1], max_c[:, u, :], AX.X, ALU.max)\
                      .then_inc(rowmax_ready, 1)
                if live(1):
                    threshold(v, 2)

            slots(dve, slot, 2)

        @block.tensor
        def _(pe):
            pe.wait_ge(consts_ready, 8)
            pe.wait_ge(weights_loaded, 48)
            nc.tensor.transpose(w_ps[:, 0:P], W_sb[:, 0:F], ident[:, :]).then_inc(WT_done, 1)
            pe.wait_ge(WT_copied, 1)
            nc.tensor.matmul(w_ps[:, P:P + 3], WT_sb[:, :], a3[:, :], start=True, stop=True)\
              .then_inc(Wa_done, 1)

            def first(s, b, loads):
                u = b % 2
                pe.wait_ge(x_loaded[b], loads * 16)
                if not isinstance(s, int) or s >= 2:
                    pe.wait_ge(xT_copied, s - 1)
                for t in range(XB):
                    last = nc.tensor.transpose(xT_ps[u][:, t * P:(t + 1) * P],
                                               x_in[:, b, t, :], ident[:, :])
                last.then_inc(xT_done, 1)
                if not isinstance(s, int) or s >= 1:
                    pe.wait_ge(xT_copied, s)
                    if not isinstance(s, int) or s >= 3:
                        pe.wait_ge(h_copied, (s - 2) * 2)
                    products_of_x(1 - u)

            def products_of_x(u):
                for t in range(XB):
                    last = nc.tensor.matmul(hs_ps[u][t // 2][:, (t % 2) * F3:(t % 2 + 1) * F3],
                                            xT[:, u, t * P:(t + 1) * P], W_sb[:, :],
                                            start=True, stop=True)
                last.then_inc(first_mm, 1)

            for s in range(NXB):
                if s == 1:
                    pe.wait_ge(Wa_copied, 1)
                first(s, s, 1)
            with pe.Fori(1, NX // NXB) as i:
                for b in range(NXB):
                    first(i * NXB + b, b, i + 1)
            pe.wait_ge(xT_copied, NX)
            pe.wait_ge(h_copied, (NX - 2) * 2)
            products_of_x((NX - 1) % 2)
            pe.wait_ge(dmax_done, 1)
            nc.tensor.transpose(k_ps[0:1, 0:P], d_max[:, 0:1], ident[:, :]).then_inc(dmaxT_done, 1)
            pe.wait_ge(dtop_done, 1)
            nc.tensor.matmul(k_ps[:, P:P + 1], ones[:, :], d_max[0:1, 1:2], start=True, stop=True)\
              .then_inc(dtop_spread, 1)
            pe.wait_ge(q_link, 2)
            nc.tensor.transpose(k_ps[0:NT, 2 * P:3 * P], q_col[:, :], ident[:, :]).then_inc(qT_done, 1)

            def transposes(k, u, g):
                n = k * NG + g
                if g % GPT == 0:
                    pe.wait_ge(thr_done, k * NTC + (g // GPT + 1))
                if not isinstance(n, int) or n >= NTR:
                    pe.wait_ge(evac_done, n + (1 - NTR))
                for b in range(GB):
                    at = g * GC + b * P
                    last = nc.tensor.transpose(tr_ps[g % NTR][:, b * P:(b + 1) * P],
                                               p_sb[:, u, at:at + P], ident[:, :])
                last.then_inc(tr_done, 1)

            def products(k, u, g):
                pe.wait_ge(evac_done, k * NG + (g + 1))
                if g == 0 and (not isinstance(k, int) or k >= 2):
                    pe.wait_ge(hp_ready, k - 1)
                for b in range(GB):
                    j = g * GB + b
                    last = nc.tensor.matmul(acc_ps[u][:, 0:F], pT[:, g % NPT, b * P:(b + 1) * P],
                                            h_sb[:, j, 0:F], start=(j == 0), stop=(j == NT - 1))
                last.then_inc(mm_done, 1)

            def slot(k, u, live):
                for c in range(NTC):
                    for i in range(GPT):
                        if live(0):
                            transposes(k, u, c * GPT + i)
                    for i in range(GPT):
                        if c == 0 and live(1):
                            products(k - 1, 1 - u, NG - GPT + i)
                        if c >= 1 and live(0):
                            products(k, u, (c - 1) * GPT + i)

            slots(pe, slot, 1, head=2)


_INS = ["x", "adj", "L0_gnn_W", "L0_gnn_a"]


def kernel(**inputs):
    import numpy as _np
    import concourse.bacc as _bacc
    from concourse import mybir as _mybir
    from concourse.bass_utils import run_bass_kernel_spmd as _run

    nc = _bacc.Bacc("TRN2", target_bir_lowering=False, num_devices=1)
    arrays, args = {}, []
    for name in _INS:
        array = _np.ascontiguousarray(inputs[name])
        arrays[f"in_{name}"] = array
        args.append(nc.dram_tensor(f"in_{name}", array.shape, _mybir.dt.from_np(array.dtype),
                                   kind="ExternalInput").ap())
    shape = inputs["x"].shape
    q_dram = nc.dram_tensor("q_dram", (shape[0] // 128, 128), _mybir.dt.float32).ap()
    out = nc.dram_tensor("out_dram", shape, _mybir.dt.float32, kind="ExternalOutput").ap()
    graph_attention_layer(nc, *args, q_dram, out)
    r = _run(nc, [arrays], core_ids=[0])
    return r.results[0]["out_dram"]
```
